# Optimizing a Trainium2 kernel written in Bass

```python
import numpy as np
import jax
import jax.numpy as jnp

def _softmax(x, axis=-1):
    return jax.nn.softmax(x, axis=axis)

def _gelu(x):
    return jax.nn.gelu(x, approximate=True)

def _silu(x):
    return jax.nn.silu(x)

def _sigmoid(x):
    return jax.nn.sigmoid(x)

def _layernorm(x, axis=-1, eps=1e-05):
    m = jnp.mean(x, axis=axis, keepdims=True)
    v = jnp.var(x, axis=axis, keepdims=True)
    return (x - m) / jnp.sqrt(v + eps)

def _scatter_add(tgt, idx, src, axis=0):
    return tgt.at[idx].add(src)

def _segment_sum(src, seg, n):
    return jax.ops.segment_sum(src, seg, n)
kernel_name = 'mk_conv_seq_d2_conv_nchw256_r2_9fb0ec'

def setup_inputs(seed: int=0):
    np.random.seed(seed)
    _w = jnp.asarray

    def _rec_inputs():
        import jax
        import jax.numpy as jnp
        _gk = jax.random.key(seed)
        x = 7.22e-05 + 1 * jax.random.normal(jax.random.fold_in(_gk, 1), (8, 128, 32, 32), jnp.float32)
        return x
    x = _rec_inputs()

    def _L0_conv_setup():
        import jax, jax.numpy as jnp
        import numpy as np
        C = 128
        C_BAR = C // 8
        key = jax.random.key(seed)
        ks = jax.random.split(key, 8)
        B, H, W = (8, 32, 32)
        s = lambda fan_in: 1.0 / np.sqrt(fan_in)
        x = jax.random.normal(ks[0], (B, C, H, W), dtype=jnp.float32)
        Wf = jax.random.normal(ks[1], (C_BAR, C), dtype=jnp.float32) * s(C)
        bf = jax.random.normal(ks[2], (C_BAR,), dtype=jnp.float32) * 0.01
        Wg = jax.random.normal(ks[3], (C_BAR, C), dtype=jnp.float32) * s(C)
        bg = jax.random.normal(ks[4], (C_BAR,), dtype=jnp.float32) * 0.01
        Wh = jax.random.normal(ks[5], (C, C), dtype=jnp.float32) * s(C)
        bh = jax.random.normal(ks[6], (C,), dtype=jnp.float32) * 0.01
        gamma = jnp.full((1,), 0.5, dtype=jnp.float32)
        return {'x': x, 'Wf': Wf, 'bf': bf, 'Wg': Wg, 'bg': bg, 'Wh': Wh, 'bh': bh, 'gamma': gamma}
    _L0_conv_all = _L0_conv_setup()
    _L0_conv_in = {k: v for k, v in _L0_conv_all.items() if k in ('Wf', 'bf', 'Wg', 'bg', 'Wh', 'bh', 'gamma')}
    del _L0_conv_all

    def _L1_conv_setup():
        import jax, jax.numpy as jnp
        import numpy as np
        NUM_GROUPS = 32
        NUM_FEATURES = 128
        EPS = 1e-05
        key = jax.random.key(seed)
        x = jax.random.normal(key, (32, NUM_FEATURES, 32, 32), dtype=jnp.float32)
        gamma = jnp.ones((NUM_FEATURES,), jnp.float32)
        beta = jnp.zeros((NUM_FEATURES,), jnp.float32)
        return {'x': x, 'gamma': gamma, 'beta': beta}
    _L1_conv_all = _L1_conv_setup()
    _L1_conv_in = {k: v for k, v in _L1_conv_all.items() if k in ('gamma', 'beta')}
    del _L1_conv_all
    return {'x': x, 'L0_conv_Wf': _L0_conv_in['Wf'], 'L0_conv_bf': _L0_conv_in['bf'], 'L0_conv_Wg': _L0_conv_in['Wg'], 'L0_conv_bg': _L0_conv_in['bg'], 'L0_conv_Wh': _L0_conv_in['Wh'], 'L0_conv_bh': _L0_conv_in['bh'], 'L0_conv_gamma': _L0_conv_in['gamma'], 'L1_conv_gamma': _L1_conv_in['gamma'], 'L1_conv_beta': _L1_conv_in['beta']}

def reference(x, L0_conv_Wf, L0_conv_bf, L0_conv_Wg, L0_conv_bg, L0_conv_Wh, L0_conv_bh, L0_conv_gamma, L1_conv_gamma, L1_conv_beta):
    import jax
    import jax.numpy as jnp

    def _L0_conv_ref(x, Wf, bf, Wg, bg, Wh, bh, gamma):
        import jax, jax.numpy as jnp
        import numpy as np
        C = 128
        C_BAR = C // 8
        B, Cc, H, W = x.shape
        N = H * W
        xf = x.reshape(B, Cc, N)
        x_f = jnp.einsum('oc,bcn->bon', Wf, xf) + bf[None, :, None]
        x_g = jnp.einsum('oc,bcn->bon', Wg, xf) + bg[None, :, None]
        x_h = jnp.einsum('oc,bcn->bon', Wh, xf) + bh[None, :, None]
        s = jnp.einsum('bci,bcj->bij', x_f, x_g)
        beta = jax.nn.softmax(s, axis=-1)
        o = jnp.einsum('bci,bij->bcj', x_h, beta).reshape(B, Cc, H, W)
        return x + gamma[0] * o

    def _L1_conv_ref(x, gamma, beta):
        import jax, jax.numpy as jnp
        import numpy as np
        NUM_GROUPS = 32
        NUM_FEATURES = 128
        EPS = 1e-05
        B, C, H, W = x.shape
        k = NUM_FEATURES // NUM_GROUPS
        x_flat = x.reshape(B, C, H * W)
        nrm = jnp.linalg.norm(x_flat, axis=2, keepdims=True)
        x_n = x_flat / jnp.maximum(nrm, 1e-12)
        cos = jnp.einsum('bcn,bdn->cd', x_n, x_n) / B
        _, idx = jax.lax.top_k(-jnp.abs(cos).T, k)
        s = x.sum(axis=(2, 3))
        sq = (x * x).sum(axis=(2, 3))
        gs = s + s[:, idx[:, 1:]].sum(axis=-1)
        gsq = sq + sq[:, idx[:, 1:]].sum(axis=-1)
        N = k * H * W
        mean = gs / N
        var = gsq / N - mean * mean
        inv = jax.lax.rsqrt(var + EPS)
        x_hat = (x - mean[:, :, None, None]) * inv[:, :, None, None]
        return gamma[None, :, None, None] * x_hat + beta[None, :, None, None]

    def _gn(v, G=32, eps=1e-05):
        B_, C_, H_, W_ = v.shape
        g = v.reshape(B_, G, C_ // G, H_, W_)
        m = jnp.mean(g, axis=(2, 3, 4), keepdims=True)
        s = jnp.var(g, axis=(2, 3, 4), keepdims=True)
        return ((g - m) / jnp.sqrt(s + eps)).reshape(v.shape)

    def _ln_c(v, eps=1e-06):
        m = jnp.mean(v, axis=1, keepdims=True)
        s = jnp.var(v, axis=1, keepdims=True)
        return (v - m) / jnp.sqrt(s + eps)

    def _ln_t(v, eps=1e-05):
        m = jnp.mean(v, axis=-1, keepdims=True)
        s = jnp.var(v, axis=-1, keepdims=True)
        return (v - m) / jnp.sqrt(s + eps)

    def _to_tokens(v):
        B_, C_, H_, W_ = v.shape
        return v.reshape(B_, C_, H_ * W_).transpose(0, 2, 1)

    def _from_tokens(t, like):
        B_, C_, H_, W_ = like.shape
        return t.transpose(0, 2, 1).reshape(B_, C_, H_, W_)
    x = _L0_conv_ref(x, L0_conv_Wf, L0_conv_bf, L0_conv_Wg, L0_conv_bg, L0_conv_Wh, L0_conv_bh, L0_conv_gamma)
    x = _L1_conv_ref(x, L1_conv_gamma, L1_conv_beta)
    return x

_drawn_inputs = setup_inputs


def setup_inputs(seed=0):
    import zlib

    import numpy as np

    out = dict(_drawn_inputs(seed))
    spreads = {'L1_conv_gamma': (1.0, 0.2), 'L1_conv_beta': (0.0, 0.1)}
    factors = {'L0_conv_bf': 5.102, 'L0_conv_bg': 8.0, 'L0_conv_bh': 3.777}
    for name, (base, spread) in spreads.items():
        noise = np.random.default_rng([zlib.crc32(name.encode()), seed]).standard_normal(out[name].shape)
        drawn = base * np.exp(spread * noise) if base else spread * noise
        out[name] = jnp.asarray(drawn.astype(out[name].dtype))
    for name, factor in factors.items():
        out[name] = (out[name] * factor).astype(out[name].dtype)
    return out
```

```python
from contextlib import ExitStack

import numpy as np

import concourse.bass as bass
from concourse import mybir

F32 = mybir.dt.float32
F32R = mybir.dt.float32r
U32 = mybir.dt.uint32
ALU = mybir.AluOpType
ACT = mybir.ActivationFunctionType
AX_X = mybir.AxisListType.X

P = 128
BANK = 512
E_SLOTS = 4
PARTNERS = 3
NORM_FLOOR = 1e-12
GN_EPS = 1e-5

WFG, WHT, BH, IDENT, IOTA, WIDE = 0, 128, 256, 384, 512, 640
C_BFG, C_NMASK, C_GAMMA, C_GNG, C_GNB, COLS = 0, 1, 2, 3, 4, 5


def build(nc, x, wide, cols, out):
    B, C, N = x.shape
    T = N // P
    H = N // BANK
    KP = 4 * 16
    assert C == P and B % 2 == 0 and T % E_SLOTS == 0

    with ExitStack() as ctx:
        def sb(name, shape, dt=F32):
            return ctx.enter_context(nc.sbuf_tensor(name, shape, dt))

        def ps(name, shape):
            return ctx.enter_context(nc.psum_tensor(name, shape, F32))

        def sem(name):
            return ctx.enter_context(nc.semaphore(name))

        x_all = sb("x_all", [P, B, N])
        y_all = sb("y_all", [P, B, N])
        x_cur = sb("x_cur", [P, N])
        wd = sb("wd", [P, WIDE])
        cl = sb("cl", [P, COLS])
        fg32 = sb("fg32", [P, N])
        fg_neg = sb("fg_neg", [P, N], F32R)
        f_parts = [sb(f"f_parts{i}", [P, N], F32R) for i in range(2)]
        g_parts = [sb(f"g_parts{i}", [P, N], F32R) for i in range(2)]
        values = [sb(f"values{i}", [P, T, P]) for i in range(2)]
        probs = [sb(f"probs{i}", [P, N]) for i in range(E_SLOTS)]
        vnorm = [sb(f"vnorm{i}", [P, P]) for i in range(E_SLOTS)]
        nmax = sb("nmax", [P, T])
        rsum = sb("rsum", [P, T])
        rinv = sb("rinv", [P, T])
        squares = sb("squares", [P, N])
        y_n = sb("y_n", [P, N])
        y_nT = sb("y_nT", [P, T, P])
        stats = sb("stats", [P, 2 * B])
        nsq = sb("nsq", [P, B])
        rnorm = sb("rnorm", [P, B])
        mhalf = sb("mhalf", [P, B])
        cos = sb("cos", [P, P])
        nabs = sb("nabs", [P, P])
        top = sb("top", [P, 8])
        top_at = sb("top_at", [P, 8], U32)
        top_f = sb("top_f", [P, 8])
        member = [sb(f"member{i}", [P, P]) for i in range(PARTNERS)]
        memberT = sb("memberT", [P, P])
        mom = sb("mom", [P, 2 * B])
        msq = sb("msq", [P, B])
        var = sb("var", [P, B])
        inv = sb("inv", [P, B])
        scl = sb("scl", [P, B])
        msc = sb("msc", [P, B])
        shf = sb("shf", [P, B])

        s_ps = [ps(f"s_ps{i}", [P, N]) for i in range(2)]
        o_ps = ps("o_ps", [P, N])
        w_ps = ps("w_ps", [P, N])

        x_in = [sem("x_in0"), sem("x_in1")]
        const_in = sem("const_in")
        cur_in = sem("cur_in")
        set_up = sem("set_up")
        fg_proj = sem("fg_proj")
        fg_copied = sem("fg_copied")
        neg_ready = sem("neg_ready")
        fg_ready = sem("fg_ready")
        v_proj = sem("v_proj")
        v_ready = sem("v_ready")
        scores = sem("scores")
        max_ready = sem("max_ready")
        exp_done = sem("exp_done")
        rinv_ready = sem("rinv_ready")
        vn_ready = sem("vn_ready")
        probs_used = sem("probs_used")
        y_ready = sem("y_ready")
        sq_ready = sem("sq_ready")
        nsq_ready = sem("nsq_ready")
        rnorm_ready = sem("rnorm_ready")
        yn_ready = sem("yn_ready")
        yT_made = sem("yT_made")
        yT_ready = sem("yT_ready")
        gram_made = sem("gram_made")
        gram_added = sem("gram_added")
        tail = sem("tail")
        member_T = sem("member_T")
        memberT_ready = sem("memberT_ready")
        mom_made = sem("mom_made")
        var_ready = sem("var_ready")
        inv_ready = sem("inv_ready")
        shift_ready = sem("shift_ready")
        v_out = sem("v_out")
        a_out = sem("a_out")
        stored = sem("stored")

        ident = wd[:, IDENT:IDENT + P]
        halves = [slice(h * BANK, (h + 1) * BANK) for h in range(H)]
        ACT_IMAGES = [b for b in range(B) if b % 3 == 2]
        VEC_IMAGES = [b for b in range(B) if b % 3 != 2]

        block = ctx.enter_context(nc.Block())

        @block.sync
        def _(sp):
            def load(b, par):
                sp.dma_start(x_all[:, b, :], x[b]).then_inc(x_in[par], 16)

            def stage(b, par, load_ahead=True, first=False):
                sp.wait_ge(v_proj, b + 1)
                sp.wait_ge(x_in[1 - par], 16 * ((b + 1 - (1 - par)) // 2 + 1) if first else 8 * (b + 1 - (1 - par)) + 16)
                sp.dma_start(x_cur[:, :], x_all[:, b + 1, :]).then_inc(cur_in, 16)
                if load_ahead:
                    load(b + 2, par)

            sp.dma_start(x_cur[:, :], x[0]).then_inc(cur_in, 16)
            sp.dma_start(cl[:, :], cols).then_inc(const_in, 16)
            load(0, 0)
            load(1, 1)
            sp.wait_ge(x_in[0], 16)
            stage(0, 0, first=True)
            with sp.Fori(0, B // 2 - 2) as i:
                for k in range(2):
                    stage(2 * i + 1 + k, 1 - k)
            stage(B - 3, 1)
            stage(B - 2, 0, load_ahead=False)
            for n, b in enumerate(VEC_IMAGES):
                sp.wait_ge(v_out, n + 1)
                sp.dma_start(out[b], y_all[:, b, :]).then_inc(stored, 16)
            sp.wait_ge(stored, 16 * B)

        @block.gpsimd
        def _(pool):
            nc.gpsimd.memset(mhalf[:, :], -0.5).then_inc(set_up, 1)
            pool.wait_ge(set_up, 5)

            for b in range(B):
                pool.wait_ge(sq_ready, b + 1)
                nc.gpsimd.tensor_scalar(nsq[:, b:b + 1], stats[:, b + B:b + B + 1], NORM_FLOOR ** 2, None,
                                        ALU.max).then_inc(nsq_ready, 1)
                pool.wait_ge(nsq_ready, b + 1)
                nc.gpsimd.tensor_tensor(rnorm[:, b:b + 1], nsq[:, b:b + 1], mhalf[:, 0:1],
                                        ALU.pow).then_inc(rnorm_ready, 1)
            pool.wait_ge(var_ready, 1)
            nc.gpsimd.tensor_tensor(inv[:, :], var[:, :], mhalf[:, :], ALU.pow).then_inc(inv_ready, 1)

        @block.scalar
        def _(act):
            act.dma_start(wd[:, :], wide).then_inc(const_in, 16)

            def copy_fg(b):
                act.wait_ge(fg_proj, b + 1)
                act.wait_ge(fg_ready, 2 * b)
                nc.scalar.activation(fg32[:, :], w_ps[:, :], ACT.Identity,
                                     bias=cl[:, C_BFG:C_BFG + 1]).then_inc(fg_copied, 1)

            def exp(g, t, fresh=False):
                act.wait_ge(max_ready, g + 1)
                if not fresh:
                    act.wait_ge(probs_used, g + 1 - E_SLOTS)
                nc.scalar.activation(probs[t % E_SLOTS][:, :], s_ps[t % 2][:, :], ACT.Exp,
                                     bias=nmax[:, t % T:t % T + 1],
                                     accum_out=rsum[:, t % T:t % T + 1]).then_inc(exp_done, 1)

            def square(b):
                act.wait_ge(y_ready, b + 1)
                nc.scalar.activation(squares[:, :], y_all[:, bass.ds(b, 1), :].rearrange("p a n -> p (a n)"),
                                     ACT.Square, accum_out=stats[:, bass.ds(b + B, 1)]).then_inc(sq_ready, 1)

            def normalise(b):
                act.wait_ge(rnorm_ready, b + 1)
                nc.scalar.activation(y_n[:, :], y_all[:, bass.ds(b, 1), :].rearrange("p a n -> p (a n)"),
                                     ACT.Copy, scale=rnorm[:, bass.ds(b, 1)]).then_inc(yn_ready, 1)

            def copy_yT(b):
                act.wait_ge(yT_made, b + 1)
                act.wait_ge(gram_added, b + 1)
                nc.scalar.activation(y_nT[:, :, :].rearrange("p t c -> p (t c)"), w_ps[:, :],
                                     ACT.Copy).then_inc(yT_ready, 1)

            def stage(b, project=True, previous=True, first=False):
                for t in range(T):
                    if project or t + 2 < T:
                        exp(b * T + t + 2, t + 2, fresh=first and t + 2 < E_SLOTS)
                    if t == 0 and previous:
                        square(b - 1)
                    if t == 1 and project:
                        copy_fg(b + 1)
                    if t == 1 and previous:
                        normalise(b - 1)
                    if t == 3 and previous:
                        copy_yT(b - 1)

            act.wait_ge(const_in, 32)
            copy_fg(0)
            exp(0, 0, fresh=True)
            exp(1, 1, fresh=True)
            stage(0, previous=False, first=True)
            with act.Fori(0, B // 2 - 1) as i:
                for k in range(2):
                    stage(2 * i + 1 + k)
            stage(B - 1, project=False)
            square(B - 1)
            normalise(B - 1)
            copy_yT(B - 1)
            act.wait_ge(shift_ready, 1)
            for n, b in enumerate(ACT_IMAGES):
                nc.scalar.activation(y_all[:, b, :], y_all[:, b, :], ACT.Identity, bias=shf[:, b:b + 1],
                                     scale=scl[:, b:b + 1]).then_inc(a_out, 1)
                act.wait_ge(a_out, n + 1)
                act.dma_start(out[b], y_all[:, b, :]).then_inc(stored, 16)

        @block.vector
        def _(dve):
            def row_max(g, t):
                dve.wait_ge(scores, g + 1)
                nc.vector.reduce_max(nmax[:, t % T:t % T + 1], s_ps[t % 2][:, :], AX_X,
                                     negate=True).then_inc(max_ready, 1)

            def normalise_values(g, t, par, fresh=False):
                dve.wait_ge(exp_done, g + 1)
                nc.vector.reciprocal(rinv[:, t:t + 1], rsum[:, t:t + 1]).then_inc(rinv_ready, 1)
                dve.wait_ge(rinv_ready, g + 1)
                if not fresh:
                    dve.wait_ge(probs_used, g + 1 - E_SLOTS)
                nc.vector.tensor_scalar(vnorm[t % E_SLOTS][:, :], values[par][:, t, :], rinv[:, t:t + 1], None,
                                        ALU.mult).then_inc(vn_ready, 1)

            def split_fg(b, par):
                dve.wait_ge(fg_copied, b + 1)
                nc.vector.tensor_scalar(fg_neg[:, :], fg32[:, :], cl[:, C_NMASK:C_NMASK + 1], None,
                                        ALU.mult).then_inc(neg_ready, 1)

            def parts_g(b, par):
                dve.wait_ge(neg_ready, b + 1)
                nc.vector.tensor_tensor(g_parts[par][0:KP, :], fg32[KP:P, :], fg_neg[KP:P, :].bitcast(F32),
                                        ALU.add).then_inc(fg_ready, 1)

            def parts_f(b, par):
                nc.vector.tensor_tensor(f_parts[par][0:KP, :], fg32[0:KP, :], fg_neg[0:KP, :].bitcast(F32),
                                        ALU.add).then_inc(fg_ready, 1)

            def add_value_bias(b, par):
                dve.wait_ge(v_proj, b + 1)
                bias = wd[:, BH:BH + P].rearrange("p (a c) -> p a c", a=1).to_broadcast([P, T, P])
                nc.vector.tensor_tensor(values[par][:, :, :], w_ps[:, :].rearrange("p (t c) -> p t c", c=P),
                                        bias, ALU.add).then_inc(v_ready, 1)

            def residual(b):
                dve.wait_ge(probs_used, T * (b + 1))
                nc.vector.scalar_tensor_tensor(y_all[:, bass.ds(b, 1), :].rearrange("p a n -> p (a n)"), o_ps[:, :],
                                               cl[:, C_GAMMA:C_GAMMA + 1],
                                               x_all[:, bass.ds(b, 1), :].rearrange("p a n -> p (a n)"),
                                               ALU.mult, ALU.add,
                                               accum_out=stats[:, bass.ds(b, 1)]).then_inc(y_ready, 1)

            def add_gram(b):
                dve.wait_ge(gram_made, b + 1)
                dve.wait_ge(gram_added, b + 1)
                nc.vector.tensor_tensor(cos[:, :], w_ps[:, 0:P], cos[:, :], ALU.add).then_inc(gram_added, 1)

            def stage(b, par, project=True, previous=True, first=False, gram=True):
                for t in range(T):
                    normalise_values(b * T + t, t, par, fresh=first and t < E_SLOTS)
                    if t == 0 and previous:
                        residual(b - 1)
                    if project or t + 2 < T:
                        row_max(b * T + t + 2, t + 2)
                    if t == 1 and gram:
                        add_gram(b - 2)
                    if project:
                        if t == 2:
                            split_fg(b + 1, 1 - par)
                            parts_g(b + 1, 1 - par)
                        if t == 3:
                            parts_f(b + 1, 1 - par)
                        if t == 6:
                            add_value_bias(b + 1, 1 - par)

            for i in range(2):
                nc.vector.memset(f_parts[i][KP:P, :].bitcast(F32), 0.0).then_inc(set_up, 1)
                nc.vector.memset(g_parts[i][KP:P, :].bitcast(F32), 0.0).then_inc(set_up, 1)
            nc.vector.memset(cos[:, :], 0.0).then_inc(gram_added, 1)
            dve.wait_ge(set_up, 5)
            dve.wait_ge(const_in, 32)
            split_fg(0, 0)
            parts_g(0, 0)
            parts_f(0, 0)
            add_value_bias(0, 0)
            row_max(0, 0)
            row_max(1, 1)
            stage(0, 0, previous=False, first=True, gram=False)
            stage(1, 1, gram=False)
            with dve.Fori(0, B // 2 - 2) as i:
                for k in range(2):
                    stage(2 * i + 2 + k, k)
            stage(B - 2, 0)
            stage(B - 1, 1, project=False)
            residual(B - 1)
            add_gram(B - 2)
            add_gram(B - 1)

            steps = [0]

            def step(instruction):
                steps[0] += 1
                instruction.then_inc(tail, 1)
                dve.wait_ge(tail, steps[0])

            dve.wait_ge(gram_added, B + 1)
            step(nc.vector.tensor_scalar(cos[:, :], cos[:, :], 1.0 / B, None, ALU.mult))
            step(nc.vector.scalar_tensor_tensor(nabs[:, :], cos[:, :], -1.0, cos[:, :], ALU.mult, ALU.min))
            step(nc.vector.max(top[:, :], nabs[:, :]))
            step(nc.vector.max_index(top_at[:, :], top[:, :], nabs[:, :]))
            step(nc.vector.tensor_copy(top_f[:, :], top_at[:, :]))
            for k in range(PARTNERS):
                step(nc.vector.scalar_tensor_tensor(member[k][:, :], wd[:, IOTA:IOTA + P], top_f[:, k + 1:k + 2],
                                                    ident if k == 0 else member[k - 1][:, :],
                                                    ALU.is_equal, ALU.add))
            dve.wait_ge(member_T, 1)
            nc.vector.tensor_copy(memberT[:, :], w_ps[:, 0:P]).then_inc(memberT_ready, 1)
            dve.wait_ge(mom_made, 1)
            step(nc.vector.tensor_scalar(mom[:, :], o_ps[:, 0:2 * B], 1.0 / ((PARTNERS + 1) * N), None, ALU.mult))
            step(nc.vector.tensor_tensor(msq[:, :], mom[:, 0:B], mom[:, 0:B], ALU.mult))
            nc.vector.scalar_tensor_tensor(var[:, :], mom[:, B:2 * B], GN_EPS, msq[:, :], ALU.add,
                                           ALU.subtract).then_inc(var_ready, 1)
            dve.wait_ge(inv_ready, 1)
            step(nc.vector.tensor_scalar(scl[:, :], inv[:, :], cl[:, C_GNG:C_GNG + 1], None, ALU.mult))
            step(nc.vector.tensor_tensor(msc[:, :], mom[:, 0:B], scl[:, :], ALU.mult))
            nc.vector.tensor_scalar(shf[:, :], msc[:, :], -1.0, cl[:, C_GNB:C_GNB + 1], ALU.mult,
                                    ALU.add).then_inc(shift_ready, 1)
            dve.wait_ge(shift_ready, 1)
            for b in VEC_IMAGES:
                nc.vector.tensor_scalar(y_all[:, b, :], y_all[:, b, :], scl[:, b:b + 1], shf[:, b:b + 1],
                                        ALU.mult, ALU.add).then_inc(v_out, 1)

        @block.tensor
        def _(pe):
            def project_fg(b, x_sem, x_count):
                pe.wait_ge(x_sem, x_count)
                for h in halves:
                    last = nc.tensor.matmul(w_ps[:, h], wd[:, WFG:WFG + P],
                                            x_all[:, bass.ds(b, 1), h].rearrange("p a n -> p (a n)"),
                                            start=True, stop=True)
                last.then_inc(fg_proj, 1)

            def project_values(b):
                pe.wait_ge(cur_in, 16 * (b + 1))
                for t in range(T):
                    last = nc.tensor.matmul(w_ps[:, t * P:(t + 1) * P], x_cur[:, t * P:(t + 1) * P],
                                            wd[:, WHT:WHT + P], start=True, stop=True)
                last.then_inc(v_proj, 1)

            def score(t, par):
                for h in halves:
                    last = nc.tensor.matmul(s_ps[t % 2][:, h], f_parts[par][:, t * P:(t + 1) * P],
                                            g_parts[par][:, h], start=True, stop=True)
                last.then_inc(scores, 1)

            def attend(g, t):
                pe.wait_ge(vn_ready, g + 1)
                for h in halves:
                    last = nc.tensor.matmul(o_ps[:, h], vnorm[t % E_SLOTS][:, :], probs[t % E_SLOTS][:, h],
                                            start=(t == 0), stop=(t == T - 1))
                last.then_inc(probs_used, 1)

            def transpose_y(b):
                pe.wait_ge(yn_ready, b + 1)
                for t in range(T):
                    last = nc.tensor.transpose(w_ps[:, t * P:(t + 1) * P], y_n[:, t * P:(t + 1) * P], ident)
                last.then_inc(yT_made, 1)

            def gram(b):
                pe.wait_ge(yT_ready, b + 1)
                for t in range(T):
                    last = nc.tensor.matmul(w_ps[:, 0:P], y_nT[:, t, :], y_nT[:, t, :], start=(t == 0),
                                            stop=(t == T - 1))
                last.then_inc(gram_made, 1)

            def stage(b, par, project=True, previous=True, x_count=None):
                for t in range(T):
                    if project or t + 2 < T:
                        pe.wait_ge(exp_done, b * T + t + 1)
                        if t + 2 == T:
                            pe.wait_ge(fg_ready, 2 * b + 4)
                        score((t + 2) % T, par if t + 2 < T else 1 - par)
                    if t == 0 and previous:
                        pe.wait_ge(y_ready, b)
                    attend(b * T + t, t)
                    if t == 1 and project:
                        if previous:
                            pe.wait_ge(gram_added, b)
                        else:
                            pe.wait_ge(v_ready, 1)
                        project_fg(b + 1, x_in[1 - par], x_count)
                    if t == 3 and previous:
                        if project:
                            pe.wait_ge(fg_copied, b + 2)
                        else:
                            pe.wait_ge(gram_added, b)
                        transpose_y(b - 1)
                    if t == 5 and project:
                        if previous:
                            pe.wait_ge(yT_ready, b)
                        else:
                            pe.wait_ge(fg_copied, 2)
                        project_values(b + 1)
                if previous:
                    if project:
                        pe.wait_ge(v_ready, b + 2)
                    gram(b - 1)

            pe.wait_ge(const_in, 32)
            project_fg(0, x_in[0], 16)
            pe.wait_ge(set_up, 5)
            pe.wait_ge(fg_copied, 1)
            project_values(0)
            pe.wait_ge(fg_ready, 2)
            score(0, 0)
            score(1, 0)
            stage(0, 0, previous=False, x_count=16)
            with pe.Fori(0, B // 2 - 1) as i:
                stage(2 * i + 1, 1, x_count=16 * i + 32)
                stage(2 * i + 2, 0, x_count=16 * i + 32)
            stage(B - 1, 1, project=False)
            pe.wait_ge(gram_added, B)
            transpose_y(B - 1)
            gram(B - 1)
            pe.wait_ge(tail, 5 + PARTNERS)
            nc.tensor.transpose(w_ps[:, 0:P], member[PARTNERS - 1][:, :], ident).then_inc(member_T, 1)
            pe.wait_ge(memberT_ready, 1)
            nc.tensor.matmul(o_ps[:, 0:2 * B], memberT[:, :], stats[:, :], start=True, stop=True).then_inc(mom_made, 1)


def kernel(x, L0_conv_Wf, L0_conv_bf, L0_conv_Wg, L0_conv_bg, L0_conv_Wh, L0_conv_bh, L0_conv_gamma,
           L1_conv_gamma, L1_conv_beta):
    import concourse.bacc as bacc
    from concourse.bass_utils import run_bass_kernel_spmd

    f32 = np.float32
    a = {k: np.asarray(v) for k, v in locals().items() if k.startswith(("x", "L"))}
    B, C, Hh, Ww = a["x"].shape
    CB = a["L0_conv_Wf"].shape[0]
    wide = np.zeros((P, WIDE), f32)
    wide[:, WFG:WFG + P] = np.concatenate([a["L0_conv_Wf"].T] * 4 + [a["L0_conv_Wg"].T] * 4, axis=1)
    wide[:, WHT:WHT + P] = a["L0_conv_Wh"].T
    wide[:, BH:BH + P] = a["L0_conv_bh"][None, :]
    wide[:, IDENT:IDENT + P] = np.eye(P, dtype=f32)
    wide[:, IOTA:IOTA + P] = np.arange(P, dtype=f32)[None, :]
    cols = np.zeros((P, COLS), f32)
    cols[:, C_BFG] = np.concatenate([a["L0_conv_bf"]] * 4 + [a["L0_conv_bg"]] * 4)
    low = np.repeat(np.array([0, 1, 0, 1, 0, 0, 1, 1], f32), CB)
    cols[:, C_NMASK] = np.where(low > 0, f32(-1), f32(0))
    cols[:, C_GAMMA] = a["L0_conv_gamma"][0]
    cols[:, C_GNG] = a["L1_conv_gamma"]
    cols[:, C_GNB] = a["L1_conv_beta"]
    arrays = {"x_dram": np.ascontiguousarray(a["x"].reshape(B, C, Hh * Ww)), "wide_dram": wide, "cols_dram": cols}

    nc = bacc.Bacc("TRN2", target_bir_lowering=False, num_devices=1)
    args = [nc.dram_tensor(k, v.shape, F32, kind="ExternalInput").ap() for k, v in arrays.items()]
    args.append(nc.dram_tensor("out_dram", (B, C, Hh * Ww), F32, kind="ExternalOutput").ap())
    build(nc, *args)
    r = run_bass_kernel_spmd(nc, [arrays], core_ids=[0])
    return r.results[0]["out_dram"].reshape(B, C, Hh, Ww)
```

```python
from contextlib import ExitStack

import numpy as np

import concourse.bass as bass
from concourse import mybir

F32 = mybir.dt.float32
F32R = mybir.dt.float32r
BF16 = mybir.dt.bfloat16
U32 = mybir.dt.uint32
ALU = mybir.AluOpType
ACT = mybir.ActivationFunctionType
AX_X = mybir.AxisListType.X

P = 128
BANK = 512
E_SLOTS = 4
PARTNERS = 3
NORM_FLOOR = 1e-12
GN_EPS = 1e-5
WARM_UPS = 8

WFG, BFG, NMASK, GAMMA, GNG, GNB, WHT = 0, 128, 129, 130, 131, 132, 133
BH, IDENT, IOTA, WIDE = WHT + 128, WHT + 256, WHT + 384, WHT + 512


def build(nc, x, wide, out):
    B, C, N = x.shape
    T = N // P
    H = N // BANK
    KP = 4 * 16
    assert C == P and B % 2 == 0 and T % E_SLOTS == 0

    with ExitStack() as ctx:
        def sb(name, shape, dt=F32):
            return ctx.enter_context(nc.sbuf_tensor(name, shape, dt))

        def ps(name, shape):
            return ctx.enter_context(nc.psum_tensor(name, shape, F32))

        def sem(name):
            return ctx.enter_context(nc.semaphore(name))

        x_all = sb("x_all", [P, B, N])
        y_all = sb("y_all", [P, B, N])
        x_cur = sb("x_cur", [P, N])
        wd = sb("wd", [P, WIDE])
        warm = sb("warm", [P, BANK], BF16)
        fg32 = sb("fg32", [P, N])
        fg_neg = sb("fg_neg", [P, N], F32R)
        f_parts = [sb(f"f_parts{i}", [P, N], F32R) for i in range(2)]
        g_parts = [sb(f"g_parts{i}", [P, N], F32R) for i in range(2)]
        values = [sb(f"values{i}", [P, T, P]) for i in range(2)]
        probs = [sb(f"probs{i}", [P, N]) for i in range(E_SLOTS)]
        vnorm = [sb(f"vnorm{i}", [P, P]) for i in range(E_SLOTS)]
        nmax = sb("nmax", [P, T])
        rsum = sb("rsum", [P, T])
        rinv = sb("rinv", [P, T])
        squares = sb("squares", [P, N])
        y_cur = sb("y_cur", [P, N])
        yT = sb("yT", [P, T, 2 * P], F32R)
        gram_high = sb("gram_high", [P, P])
        gram_rows = sb("gram_rows", [P, P])
        sums = sb("sums", [P, H, B])
        last_sq = sb("last_sq", [P, H])
        stats = sb("stats", [P, 2 * B])
        nsq = sb("nsq", [P, B])
        rnorm = sb("rnorm", [P, B])
        mhalf = sb("mhalf", [P, B])
        cos = sb("cos", [P, P])
        half_cos = sb("half_cos", [P, P])
        half_mean = sb("half_mean", [P, P])
        nabs = sb("nabs", [P, P])
        top = sb("top", [P, 8])
        top_at = sb("top_at", [P, 8], U32)
        top_f = sb("top_f", [P, 8])
        member = [sb(f"member{i}", [P, P]) for i in range(PARTNERS)]
        memberT = sb("memberT", [P, P])
        mom = sb("mom", [P, 2 * B])
        msq = sb("msq", [P, B])
        var = sb("var", [P, B])
        inv = sb("inv", [P, B])
        scl = sb("scl", [P, B])
        msc = sb("msc", [P, B])
        shf = sb("shf", [P, B])

        s_ps = [ps(f"s_ps{i}", [P, N]) for i in range(2)]
        o_ps = ps("o_ps", [P, N])
        w_ps = ps("w_ps", [P, N])

        head_in = [sem("head_in0"), sem("head_in1")]
        x_in = [sem("x_in0"), sem("x_in1")]
        table_in = sem("table_in")
        wfg_in = sem("wfg_in")
        const_in = sem("const_in")
        cur_in = sem("cur_in")
        warm_set = sem("warm_set")
        halves_set = sem("halves_set")
        zeros_set = sem("zeros_set")
        fg_proj = sem("fg_proj")
        fg_copied = sem("fg_copied")
        neg_ready = sem("neg_ready")
        g_ready = sem("g_ready")
        f_ready = sem("f_ready")
        f_head = sem("f_head")
        v_proj = sem("v_proj")
        v_ready = sem("v_ready")
        scores = sem("scores")
        max_ready = sem("max_ready")
        exp_done = sem("exp_done")
        rinv_ready = sem("rinv_ready")
        vn_ready = sem("vn_ready")
        probs_used = sem("probs_used")
        y_ready = sem("y_ready")
        y_kept = sem("y_kept")
        sq_ready = sem("sq_ready")
        sums_ready = sem("sums_ready")
        nsq_ready = sem("nsq_ready")
        rnorm_ready = sem("rnorm_ready")
        yT_made = sem("yT_made")
        yT_high = sem("yT_high")
        yT_ready = sem("yT_ready")
        gram_made = sem("gram_made")
        gram_half = sem("gram_half")
        gram_scaled = sem("gram_scaled")
        gram_turned = sem("gram_turned")
        gram_added = sem("gram_added")
        half_turned = sem("half_turned")
        tail = sem("tail")
        member_T = sem("member_T")
        memberT_ready = sem("memberT_ready")
        mom_made = sem("mom_made")
        var_ready = sem("var_ready")
        inv_ready = sem("inv_ready")
        shift_ready = sem("shift_ready")
        v_out = sem("v_out")
        a_out = sem("a_out")
        stored = sem("stored")

        ident = wd[:, IDENT:IDENT + P]
        halves = [slice(h * BANK, (h + 1) * BANK) for h in range(H)]
        TH = T // H
        L = B - 1
        ACT_IMAGES = [b for b in range(B) if b % 3 == 2]
        VEC_IMAGES = [b for b in range(B) if b % 3 != 2]

        def image(stack, b):
            return stack[:, bass.ds(b, 1), :].rearrange("p a n -> p (a n)")

        def run_stages(engine, stage):
            stage(0, 0, first=True, previous=False, turn=False)
            stage(1, 1, turn=False)
            with engine.Fori(0, B // 2 - 2) as i:
                stage(2 * i + 2, 0, x_count=16 * i + 32)
                stage(2 * i + 3, 1, x_count=16 * i + 32)
            stage(B - 2, 0, load_ahead=False, x_count=8 * B)
            stage(B - 1, 1, project=False)

        block = ctx.enter_context(nc.Block())

        @block.sync
        def _(sp):
            def load(b, par):
                sp.dma_start(x_all[:, b, :], x[b]).then_inc(x_in[par], 16)

            def stage(b, par, first=False, previous=True, turn=True, project=True, load_ahead=True, x_count=16):
                if project:
                    sp.wait_ge(v_proj, H * (b + 1))
                    sp.wait_ge(x_in[1 - par], x_count)
                    sp.dma_start(x_cur[:, :], x_all[:, b + 1, :]).then_inc(cur_in, 16)
                    if load_ahead:
                        load(b + 2, par)
                if previous:
                    sp.wait_ge(y_ready, H * b)
                    sp.dma_start(y_all[:, b - 1, :], y_cur[:, :]).then_inc(y_kept, 16)

            for h in range(H):
                sp.dma_start(x_all[:, 0, halves[h]], x[0][:, halves[h]]).then_inc(head_in[h], 16)
            load(1, 1)
            run_stages(sp, stage)
            for n, b in enumerate(VEC_IMAGES):
                sp.wait_ge(v_out, n + 1)
                sp.dma_start(out[b], y_all[:, b, :]).then_inc(stored, 16)
            sp.wait_ge(stored, 16 * B)

        @block.gpsimd
        def _(pool):
            nc.gpsimd.memset(mhalf[:, :], -0.5).then_inc(halves_set, 1)
            pool.wait_ge(halves_set, 1)
            def parts_f(b):
                for h in range(H):
                    pool.wait_ge(neg_ready, H * b + h + 1)
                    if b >= 2:
                        pool.wait_ge(scores, T * (b - 1))
                    nc.gpsimd.tensor_tensor(f_parts[b % 2][0:KP, halves[h]], fg32[0:KP, halves[h]],
                                            fg_neg[0:KP, halves[h]].bitcast(F32), ALU.add).then_inc(f_ready, 1)

            for b in range(B):
                if b == 0:
                    parts_f(1)
                if b + 2 < B:
                    parts_f(b + 2)
                if b < L:
                    pool.wait_ge(sq_ready, b + 1)
                else:
                    pool.wait_ge(sums_ready, 1)
                nc.gpsimd.tensor_scalar(nsq[:, b:b + 1], stats[:, b + B:b + B + 1], NORM_FLOOR ** 2, None,
                                        ALU.max).then_inc(nsq_ready, 1)
                pool.wait_ge(nsq_ready, b + 1)
                nc.gpsimd.tensor_tensor(rnorm[:, b:b + 1], nsq[:, b:b + 1], mhalf[:, 0:1],
                                        ALU.pow).then_inc(rnorm_ready, 1)
            pool.wait_ge(table_in, 1)
            pool.wait_ge(var_ready, 1)
            nc.gpsimd.tensor_tensor(inv[:, :], var[:, :], mhalf[:, :], ALU.pow).then_inc(inv_ready, 1)

        @block.scalar
        def _(act):
            act.dma_start(wd[:, 0:WHT], wide[:, 0:WHT]).then_inc(wfg_in, 16)
            act.dma_start(wd[:, WHT:WIDE], wide[:, WHT:WIDE]).then_inc(const_in, 16)

            act.wait_ge(halves_set, 1)
            nc.scalar.activation(inv[:, 0:1], mhalf[:, 0:1], ACT.Exp).then_inc(table_in, 1)

            def copy_fg(b, h):
                act.wait_ge(fg_proj, H * b + h + 1)
                nc.scalar.activation(fg32[:, halves[h]], w_ps[:, halves[h]], ACT.Identity,
                                     bias=wd[:, BFG:BFG + 1]).then_inc(fg_copied, 1)
                act.wait_ge(fg_copied, H * b + h + 1)
                nc.scalar.activation(fg_neg[:, halves[h]], fg32[:, halves[h]], ACT.Copy,
                                     scale=wd[:, NMASK:NMASK + 1]).then_inc(neg_ready, 1)

            def exp(g, t, fresh=False):
                act.wait_ge(max_ready, g + 1)
                if not fresh:
                    act.wait_ge(probs_used, g + 1 - E_SLOTS)
                nc.scalar.activation(probs[t % E_SLOTS][:, :], s_ps[t % 2][:, :], ACT.Exp,
                                     bias=nmax[:, t % T:t % T + 1],
                                     accum_out=rsum[:, t % T:t % T + 1]).then_inc(exp_done, 1)

            def stage(b, par, first=False, previous=True, turn=True, project=True, load_ahead=True, x_count=16):
                for t in range(T):
                    if project or t + 2 < T:
                        exp(b * T + t + 2, t + 2, fresh=first and t + 2 < E_SLOTS)
                    if t == 0 and previous:
                        act.wait_ge(y_ready, H * b)
                        nc.scalar.activation(squares[:, :], y_cur[:, :], ACT.Square,
                                             accum_out=stats[:, bass.ds(b - 1 + B, 1)]).then_inc(sq_ready, 1)
                    if t == 1 and project:
                        act.wait_ge(g_ready, H * (b + 1))
                        if first:
                            act.wait_ge(f_head, H)
                        else:
                            act.wait_ge(f_ready, H * b)
                        copy_fg(b + 1, 0)
                    if t == 2 and project:
                        copy_fg(b + 1, 1)
                    if t == 3 and previous:
                        act.wait_ge(yT_made, b)
                        nc.scalar.activation(yT[:, :, 0:P], w_ps[:, :].rearrange("p (t c) -> p t c", c=P),
                                             ACT.Copy).then_inc(yT_high, 1)

            act.wait_ge(wfg_in, 16)
            for h in range(H):
                copy_fg(0, h)
            exp(0, 0, fresh=True)
            exp(1, 1, fresh=True)
            run_stages(act, stage)
            act.wait_ge(y_ready, H * L + 1)
            nc.scalar.activation(squares[:, halves[0]], y_all[:, L, halves[0]], ACT.Square,
                                 accum_out=last_sq[:, 0:1]).then_inc(sq_ready, 1)
            act.wait_ge(gram_made, L)
            for h in range(H):
                act.wait_ge(yT_made, L + 1 + h)
                nc.scalar.activation(yT[:, h * TH:(h + 1) * TH, 0:P],
                                     s_ps[h][:, halves[0]].rearrange("p (t c) -> p t c", c=P),
                                     ACT.Copy).then_inc(yT_high, 1)
            act.wait_ge(y_ready, H * B)
            nc.scalar.activation(squares[:, halves[1]], y_all[:, L, halves[1]], ACT.Square,
                                 accum_out=last_sq[:, 1:2]).then_inc(sq_ready, 1)
            act.wait_ge(shift_ready, 1)
            act.wait_ge(y_kept, 16 * L)
            for n, b in enumerate(ACT_IMAGES):
                nc.scalar.activation(y_all[:, b, :], y_all[:, b, :], ACT.Identity, bias=shf[:, b:b + 1],
                                     scale=scl[:, b:b + 1]).then_inc(a_out, 1)
                act.wait_ge(a_out, n + 1)
                act.dma_start(out[b], y_all[:, b, :]).then_inc(stored, 16)

        @block.vector
        def _(dve):
            def row_max(g, t):
                dve.wait_ge(scores, g + 1)
                nc.vector.reduce_max(nmax[:, t % T:t % T + 1], s_ps[t % 2][:, :], AX_X,
                                     negate=True).then_inc(max_ready, 1)

            def normalise_values(g, t, par, fresh=False):
                dve.wait_ge(exp_done, g + 1)
                nc.vector.reciprocal(rinv[:, t:t + 1], rsum[:, t:t + 1]).then_inc(rinv_ready, 1)
                dve.wait_ge(rinv_ready, g + 1)
                if not fresh:
                    dve.wait_ge(probs_used, g + 1 - E_SLOTS)
                nc.vector.tensor_scalar(vnorm[t % E_SLOTS][:, :], values[par][:, t, :], rinv[:, t:t + 1], None,
                                        ALU.mult).then_inc(vn_ready, 1)

            def parts(to, rows, columns, done):
                nc.vector.tensor_tensor(to[0:KP, columns], fg32[rows, columns], fg_neg[rows, columns].bitcast(F32),
                                        ALU.add).then_inc(done, 1)

            f_rows, g_rows = slice(0, KP), slice(KP, P)

            def add_value_bias(b, par, h, source):
                dve.wait_ge(v_proj, H * b + h + 1)
                bias = wd[:, BH:BH + P].rearrange("p (a c) -> p a c", a=1).to_broadcast([P, TH, P])
                nc.vector.tensor_tensor(values[par][:, h * TH:(h + 1) * TH, :],
                                        source[:, halves[h]].rearrange("p (t c) -> p t c", c=P),
                                        bias, ALU.add).then_inc(v_ready, 1)

            def residual(b, first):
                dve.wait_ge(probs_used, T * (b + 1))
                if not first:
                    dve.wait_ge(y_kept, 16 * b)
                    dve.wait_ge(sq_ready, b)
                    dve.wait_ge(yT_made, b)
                for h in range(H):
                    nc.vector.scalar_tensor_tensor(y_cur[:, halves[h]], o_ps[:, halves[h]], wd[:, GAMMA:GAMMA + 1],
                                                   image(x_all, b)[:, halves[h]], ALU.mult, ALU.add,
                                                   accum_out=sums[:, h, bass.ds(b, 1)]).then_inc(y_ready, 1)

            def low_part(tiles, source):
                nc.vector.tensor_tensor(yT[:, tiles, P:2 * P], source.rearrange("p (t c) -> p t c", c=P),
                                        yT[:, tiles, 0:P].bitcast(F32), ALU.subtract).then_inc(yT_ready, 1)

            def scale_gram(b, product):
                dve.wait_ge(gram_made, b + 1)
                dve.wait_ge(rnorm_ready, b + 1)
                nc.vector.tensor_scalar(gram_high[:, :], product[:, 0:P], rnorm[:, bass.ds(b, 1)], 0.5,
                                        ALU.mult, ALU.mult).then_inc(gram_half, 1)
                dve.wait_ge(gram_half, b + 1)
                nc.vector.scalar_tensor_tensor(gram_rows[:, :], product[:, P:2 * P], rnorm[:, bass.ds(b, 1)],
                                               gram_high[:, :], ALU.mult, ALU.add).then_inc(gram_scaled, 1)

            def add_gram(b, turned):
                dve.wait_ge(gram_turned, b + 1)
                dve.wait_ge(gram_added, b + 1)
                nc.vector.scalar_tensor_tensor(half_cos[:, :], turned, rnorm[:, bass.ds(b, 1)], half_cos[:, :],
                                               ALU.mult, ALU.add).then_inc(gram_added, 1)

            def stage(b, par, first=False, previous=True, turn=True, project=True, load_ahead=True, x_count=16):
                for t in range(T):
                    if t == 0 and previous:
                        residual(b - 1, first=not turn)
                    if t == 2 and turn:
                        add_gram(b - 2, w_ps[:, BANK:BANK + P])
                    if project or t + 2 < T:
                        row_max(b * T + t + 2, t + 2)
                    if project or t + 1 < T:
                        normalise_values(b * T + t + 1, (t + 1) % T, par if t + 1 < T else 1 - par,
                                         fresh=first and t + 1 < E_SLOTS)
                    if t == 0 and turn:
                        scale_gram(b - 2, w_ps)
                    if t in (2, 3) and project:
                        dve.wait_ge(neg_ready, H * (b + 1) + t - 1)
                        parts(g_parts[1 - par], g_rows, halves[t - 2], g_ready)
                    if t in (4, 5) and previous:
                        h = t - 4
                        dve.wait_ge(yT_high, b)
                        low_part(slice(h * TH, (h + 1) * TH), w_ps[:, halves[h]])
                    if t in (6, 7) and project:
                        add_value_bias(b + 1, 1 - par, t - 6, w_ps)

            nc.vector.memset(warm[:, :], 0.0).then_inc(warm_set, 1)
            for i in range(2):
                nc.vector.memset(f_parts[i][KP:P, :].bitcast(F32), 0.0).then_inc(zeros_set, 1)
                nc.vector.memset(g_parts[i][KP:P, :].bitcast(F32), 0.0).then_inc(zeros_set, 1)
            nc.vector.memset(half_cos[:, :], 0.0).then_inc(gram_added, 1)
            dve.wait_ge(wfg_in, 16)
            for h in range(H):
                dve.wait_ge(neg_ready, h + 1)
                parts(g_parts[0], g_rows, halves[h], g_ready)
                if h == 0:
                    parts(f_parts[0], f_rows, halves[0], f_head)
            parts(f_parts[0], f_rows, halves[1], f_head)
            row_max(0, 0)
            row_max(1, 1)
            dve.wait_ge(const_in, 16)
            for h in range(H):
                add_value_bias(0, 0, h, o_ps)
            normalise_values(0, 0, 0, fresh=True)
            run_stages(dve, stage)
            dve.wait_ge(probs_used, T * B)
            for h in range(H):
                nc.vector.scalar_tensor_tensor(y_all[:, L, halves[h]], o_ps[:, halves[h]], wd[:, GAMMA:GAMMA + 1],
                                               x_all[:, L, halves[h]], ALU.mult, ALU.add,
                                               accum_out=sums[:, h, L:L + 1]).then_inc(y_ready, 1)
            scale_gram(L - 1, w_ps)
            for h in range(H):
                dve.wait_ge(yT_high, L + 1 + h)
                low_part(slice(h * TH, (h + 1) * TH), s_ps[h][:, halves[0]])
            add_gram(L - 1, w_ps[:, BANK:BANK + P])
            dve.wait_ge(sq_ready, L + 2)
            nc.vector.tensor_tensor(stats[:, 2 * B - 1:2 * B], last_sq[:, 0:1], last_sq[:, 1:2],
                                    ALU.add).then_inc(sums_ready, 1)
            dve.wait_ge(y_ready, H * B)
            nc.vector.tensor_tensor(stats[:, 0:B], sums[:, 0, :], sums[:, 1, :], ALU.add).then_inc(sums_ready, 1)
            scale_gram(L, o_ps)
            add_gram(L, o_ps[:, BANK:BANK + P])

            steps = [0]

            def step(instruction):
                steps[0] += 1
                instruction.then_inc(tail, 1)
                dve.wait_ge(tail, steps[0])

            dve.wait_ge(gram_added, B + 1)
            step(nc.vector.tensor_scalar(half_mean[:, :], half_cos[:, :], 1.0 / B, None, ALU.mult))
            dve.wait_ge(half_turned, 1)
            step(nc.vector.scalar_tensor_tensor(cos[:, :], s_ps[0][:, BANK:BANK + P], 1.0 / B, half_mean[:, :],
                                                ALU.mult, ALU.add))
            step(nc.vector.scalar_tensor_tensor(nabs[:, :], cos[:, :], -1.0, cos[:, :], ALU.mult, ALU.min))
            step(nc.vector.max(top[:, :], nabs[:, :]))
            step(nc.vector.max_index(top_at[:, :], top[:, :], nabs[:, :]))
            step(nc.vector.tensor_copy(top_f[:, :], top_at[:, :]))
            for k in range(PARTNERS):
                step(nc.vector.scalar_tensor_tensor(member[k][:, :], wd[:, IOTA:IOTA + P], top_f[:, k + 1:k + 2],
                                                    ident if k == 0 else member[k - 1][:, :],
                                                    ALU.is_equal, ALU.add))
            dve.wait_ge(member_T, 1)
            nc.vector.tensor_copy(memberT[:, :], w_ps[:, 0:P]).then_inc(memberT_ready, 1)
            dve.wait_ge(mom_made, 1)
            step(nc.vector.tensor_scalar(mom[:, :], o_ps[:, 0:2 * B], 1.0 / ((PARTNERS + 1) * N), None, ALU.mult))
            step(nc.vector.tensor_tensor(msq[:, :], mom[:, 0:B], mom[:, 0:B], ALU.mult))
            nc.vector.scalar_tensor_tensor(var[:, :], mom[:, B:2 * B], GN_EPS, msq[:, :], ALU.add,
                                           ALU.subtract).then_inc(var_ready, 1)
            dve.wait_ge(inv_ready, 1)
            step(nc.vector.tensor_scalar(scl[:, :], inv[:, :], wd[:, GNG:GNG + 1], None, ALU.mult))
            step(nc.vector.tensor_tensor(msc[:, :], mom[:, 0:B], scl[:, :], ALU.mult))
            nc.vector.tensor_scalar(shf[:, :], msc[:, :], -1.0, wd[:, GNB:GNB + 1], ALU.mult,
                                    ALU.add).then_inc(shift_ready, 1)
            dve.wait_ge(shift_ready, 1)
            dve.wait_ge(y_kept, 16 * L)
            for b in VEC_IMAGES:
                nc.vector.tensor_scalar(y_all[:, b, :], y_all[:, b, :], scl[:, b:b + 1], shf[:, b:b + 1],
                                        ALU.mult, ALU.add).then_inc(v_out, 1)

        @block.tensor
        def _(pe):
            def keep_warm(to):
                for _ in range(WARM_UPS):
                    nc.tensor.matmul(to[:, halves[0]], warm[:, 0:P], warm[:, :], start=True, stop=True)

            def project_fg(b, h):
                return nc.tensor.matmul(w_ps[:, halves[h]], wd[:, WFG:WFG + P], image(x_all, b)[:, halves[h]],
                                        start=True, stop=True)

            def project_values(source, to, h):
                for t in range(h * TH, (h + 1) * TH):
                    last = nc.tensor.matmul(to[:, t * P:(t + 1) * P], source[:, t * P:(t + 1) * P],
                                            wd[:, WHT:WHT + P], start=True, stop=True)
                last.then_inc(v_proj, 1)

            def score(t, par):
                for h in halves:
                    last = nc.tensor.matmul(s_ps[t % 2][:, h], f_parts[par][:, t * P:(t + 1) * P],
                                            g_parts[par][:, h], start=True, stop=True)
                last.then_inc(scores, 1)

            def attend(g, t, after=None):
                pe.wait_ge(vn_ready, g + 1)
                for h in range(H):
                    if after is not None:
                        pe.wait_ge(y_ready, H * (after - 1) + h + 1)
                    last = nc.tensor.matmul(o_ps[:, halves[h]], vnorm[t % E_SLOTS][:, :],
                                            probs[t % E_SLOTS][:, halves[h]],
                                            start=(t == 0), stop=(t == T - 1))
                last.then_inc(probs_used, 1)

            def transposes(source, to, tiles, first=0):
                for t in tiles:
                    last = nc.tensor.transpose(to[:, (t - first) * P:(t - first + 1) * P], source[:, t * P:(t + 1) * P], ident)
                last.then_inc(yT_made, 1)

            def gram(to, tiles):
                for t in tiles:
                    last = nc.tensor.matmul(to[:, 0:2 * P], yT[:, t, 0:P], yT[:, t, :], start=(t == 0),
                                            stop=(t == T - 1))
                return last

            def turn_gram(b, to):
                pe.wait_ge(gram_scaled, b + 1)
                nc.tensor.transpose(to, gram_rows[:, :], ident).then_inc(gram_turned, 1)

            def stage(b, par, first=False, previous=True, turn=True, project=True, load_ahead=True, x_count=16):
                for t in range(T):
                    if project or t + 2 < T:
                        pe.wait_ge(exp_done, b * T + t + 1)
                        if t + 2 == T:
                            pe.wait_ge(g_ready, H * (b + 2))
                            pe.wait_ge(f_ready, H * b + 1)
                        if t == 2:
                            if first:
                                pe.wait_ge(f_head, H)
                            else:
                                pe.wait_ge(f_ready, H * b)
                        score((t + 2) % T, par if t + 2 < T else 1 - par)
                    if first and t == 0:
                        keep_warm(w_ps)
                    attend(b * T + t, t, b if t == 0 and previous else None)
                    if t == 1 and turn:
                        turn_gram(b - 2, w_ps[:, BANK:BANK + P])
                    if t == 1 and project:
                        if first:
                            pe.wait_ge(fg_copied, H)
                        pe.wait_ge(x_in[1 - par], x_count)
                        for h in range(H):
                            if h == 1 and turn:
                                pe.wait_ge(gram_added, b)
                            project_fg(b + 1, h).then_inc(fg_proj, 1)
                    if t == 3 and previous:
                        if project:
                            pe.wait_ge(fg_copied, H * (b + 2))
                        else:
                            pe.wait_ge(gram_added, b)
                        transposes(y_cur, w_ps, range(T))
                    if t == 5 and project:
                        pe.wait_ge(cur_in, 16 * (b + 1))
                        for h in range(H):
                            if previous:
                                pe.wait_ge(yT_ready, H * (b - 1) + h + 1)
                            else:
                                pe.wait_ge(fg_copied, 2 * H)
                            project_values(x_cur, w_ps, h)
                if previous:
                    if project:
                        pe.wait_ge(v_ready, H * (b + 1) + 1)
                    pe.wait_ge(yT_ready, H * b)
                    gram(w_ps, range(T)).then_inc(gram_made, 1)

            pe.wait_ge(warm_set, 1)
            keep_warm(o_ps)
            pe.wait_ge(wfg_in, 16)
            for h in range(H):
                pe.wait_ge(head_in[h], 16)
                project_fg(0, h).then_inc(fg_proj, 1)
            pe.wait_ge(const_in, 16)
            for h in range(H):
                project_values(x_all[:, 0, :], o_ps, h)
            pe.wait_ge(zeros_set, 4)
            pe.wait_ge(g_ready, H)
            pe.wait_ge(f_head, 1)
            score(0, 0)
            score(1, 0)
            keep_warm(w_ps)
            run_stages(pe, stage)
            for h in range(H):
                pe.wait_ge(y_ready, H * L + 1 + h)
                transposes(y_all[:, L, :], s_ps[h], range(h * TH, (h + 1) * TH), first=h * TH)
                if h == 0:
                    turn_gram(L - 1, w_ps[:, BANK:BANK + P])
            for h in range(H):
                pe.wait_ge(yT_ready, H * L + 1 + h)
                last = gram(o_ps, range(h * TH, (h + 1) * TH))
            last.then_inc(gram_made, 1)
            turn_gram(L, o_ps[:, BANK:BANK + P])
            pe.wait_ge(gram_added, B + 1)
            nc.tensor.transpose(s_ps[0][:, BANK:BANK + P], half_cos[:, :], ident).then_inc(half_turned, 1)
            pe.wait_ge(tail, 6 + PARTNERS)
            nc.tensor.transpose(w_ps[:, 0:P], member[PARTNERS - 1][:, :], ident).then_inc(member_T, 1)
            pe.wait_ge(memberT_ready, 1)
            pe.wait_ge(sums_ready, 2)
            nc.tensor.matmul(o_ps[:, 0:2 * B], memberT[:, :], stats[:, :], start=True, stop=True).then_inc(mom_made, 1)


def kernel(x, L0_conv_Wf, L0_conv_bf, L0_conv_Wg, L0_conv_bg, L0_conv_Wh, L0_conv_bh, L0_conv_gamma,
           L1_conv_gamma, L1_conv_beta):
    import concourse.bacc as bacc
    from concourse.bass_utils import run_bass_kernel_spmd

    f32 = np.float32
    a = {k: np.asarray(v) for k, v in locals().items() if k.startswith(("x", "L"))}
    B, C, Hh, Ww = a["x"].shape
    CB = a["L0_conv_Wf"].shape[0]
    wide = np.zeros((P, WIDE), f32)
    wide[:, WFG:WFG + P] = np.concatenate([a["L0_conv_Wf"].T] * 4 + [a["L0_conv_Wg"].T] * 4, axis=1)
    wide[:, WHT:WHT + P] = a["L0_conv_Wh"].T
    wide[:, BH:BH + P] = a["L0_conv_bh"][None, :]
    wide[:, IDENT:IDENT + P] = np.eye(P, dtype=f32)
    wide[:, IOTA:IOTA + P] = np.arange(P, dtype=f32)[None, :]
    wide[:, BFG] = np.concatenate([a["L0_conv_bf"]] * 4 + [a["L0_conv_bg"]] * 4)
    low = np.repeat(np.array([0, 1, 0, 1, 0, 0, 1, 1], f32), CB)
    wide[:, NMASK] = np.where(low > 0, f32(-1), f32(0))
    wide[:, GAMMA] = a["L0_conv_gamma"][0]
    wide[:, GNG] = a["L1_conv_gamma"]
    wide[:, GNB] = a["L1_conv_beta"]
    arrays = {"x_dram": np.ascontiguousarray(a["x"].reshape(B, C, Hh * Ww)), "wide_dram": wide}

    nc = bacc.Bacc("TRN2", target_bir_lowering=False, num_devices=1)
    args = [nc.dram_tensor(k, v.shape, F32, kind="ExternalInput").ap() for k, v in arrays.items()]
    args.append(nc.dram_tensor("out_dram", (B, C, Hh * Ww), F32, kind="ExternalOutput").ap())
    build(nc, *args)
    r = run_bass_kernel_spmd(nc, [arrays], core_ids=[0])
    return r.results[0]["out_dram"].reshape(B, C, Hh, Ww)
```

```python
from contextlib import ExitStack

import numpy as np

import concourse.bass as bass
from concourse import mybir

F32 = mybir.dt.float32
F32R = mybir.dt.float32r
BF16 = mybir.dt.bfloat16
U32 = mybir.dt.uint32
ALU = mybir.AluOpType
ACT = mybir.ActivationFunctionType
AX_X = mybir.AxisListType.X

P = 128
BANK = 512
AHEAD = 3
SCALED = 2
SPLIT = (3, 7)
PARTNERS = 3
NORM_FLOOR = 1e-12
GN_EPS = 1e-5
WARM_UPS = 8

WFG, BFG, NMASK, GAMMA, GNG, GNB, WHT = 0, 128, 129, 130, 131, 132, 133
BH, IDENT, IOTA, WIDE = WHT + 128, WHT + 256, WHT + 384, WHT + 512


def build(nc, x, wide, out):
    B, C, N = x.shape
    T = N // P
    H = N // BANK
    KP = 4 * 16
    assert C == P and H == 2 and T == 8 and B % 2 == 0 and B >= 4
    assert all(SCALED <= t < T for t in SPLIT)

    with ExitStack() as ctx:
        def sb(name, shape, dt=F32):
            return ctx.enter_context(nc.sbuf_tensor(name, shape, dt))

        def ps(name, shape):
            return ctx.enter_context(nc.psum_tensor(name, shape, F32))

        def sem(name):
            return ctx.enter_context(nc.semaphore(name))

        x_all = sb("x_all", [P, B, N])
        y_all = sb("y_all", [P, B, N])
        x_cur = sb("x_cur", [P, N])
        wd = sb("wd", [P, WIDE])
        warm = sb("warm", [P, BANK], BF16)
        fg32 = sb("fg32", [P, N])
        fg_neg = sb("fg_neg", [P, N], F32R)
        f_parts = [sb(f"f_parts{i}", [P, N], F32R) for i in range(2)]
        g_parts = [sb(f"g_parts{i}", [P, N], F32R) for i in range(2)]
        values = [sb(f"values{i}", [P, T, P]) for i in range(2)]
        probs = [sb(f"probs{i}", [P, N]) for i in range(T)]
        vnorm = [sb(f"vnorm{i}", [P, P]) for i in range(T)]
        probs_high = [sb(f"probs_high{i}", [P, N], F32R) for i in range(len(SPLIT))]
        probs_low = [sb(f"probs_low{i}", [P, N], F32R) for i in range(len(SPLIT))]
        v_high = [sb(f"v_high{i}", [P, P], F32R) for i in range(len(SPLIT))]
        v_low = [sb(f"v_low{i}", [P, P], F32R) for i in range(len(SPLIT))]
        nmax = sb("nmax", [P, T])
        rsum = sb("rsum", [P, T])
        rinv = sb("rinv", [P, T])
        squares = sb("squares", [P, N])
        y_cur = sb("y_cur", [P, N])
        yT = sb("yT", [P, T, 2 * P], F32R)
        gram_high = sb("gram_high", [P, P])
        gram_rows = sb("gram_rows", [P, P])
        sums = sb("sums", [P, H, B])
        last_sq = sb("last_sq", [P, H])
        stats = sb("stats", [P, 2 * B])
        nsq = sb("nsq", [P, B])
        rnorm = sb("rnorm", [P, B])
        mhalf = sb("mhalf", [P, B])
        cos = sb("cos", [P, P])
        half_cos = sb("half_cos", [P, P])
        half_mean = sb("half_mean", [P, P])
        nabs = sb("nabs", [P, P])
        top = sb("top", [P, 8])
        top_at = sb("top_at", [P, 8], U32)
        partner = sb("partner", [P, PARTNERS, P], BF16)
        ident_b = sb("ident_b", [P, P], BF16)
        memberT = sb("memberT", [P, P])
        shares = sb("shares", [P, 2 * B])
        mean = sb("mean", [P, B])
        msq = sb("msq", [P, B])
        var = sb("var", [P, B])
        inv = sb("inv", [P, B])
        scl = sb("scl", [P, B])
        msc = sb("msc", [P, B])
        minv = sb("minv", [P, B])
        shf = sb("shf", [P, B])

        s_ps = [ps(f"s_ps{i}", [P, N]) for i in range(2)]
        o_ps = ps("o_ps", [P, N])
        w_ps = ps("w_ps", [P, N])

        head_in = [sem("head_in0"), sem("head_in1")]
        x_in = [sem("x_in0"), sem("x_in1")]
        table_in = sem("table_in")
        wfg_in = sem("wfg_in")
        const_in = sem("const_in")
        cur_in = sem("cur_in")
        warm_set = sem("warm_set")
        halves_set = sem("halves_set")
        zeros_set = sem("zeros_set")
        fg_proj = sem("fg_proj")
        fg_copied = sem("fg_copied")
        neg_ready = sem("neg_ready")
        g_ready = sem("g_ready")
        f_head = sem("f_head")
        f_ready = sem("f_ready")
        v_proj = sem("v_proj")
        v_ready = sem("v_ready")
        scores = sem("scores")
        max_ready = sem("max_ready")
        exp_done = sem("exp_done")
        rinv_ready = sem("rinv_ready")
        high_ready = sem("high_ready")
        low_ready = sem("low_ready")
        vh_ready = sem("vh_ready")
        vl_ready = sem("vl_ready")
        vn_ready = sem("vn_ready")
        first_half = sem("first_half")
        probs_used = sem("probs_used")
        y_ready = sem("y_ready")
        y_kept = sem("y_kept")
        sq_ready = sem("sq_ready")
        sums_ready = sem("sums_ready")
        nsq_ready = sem("nsq_ready")
        rnorm_ready = sem("rnorm_ready")
        yT_made = sem("yT_made")
        yT_high = sem("yT_high")
        yT_ready = sem("yT_ready")
        gram_made = sem("gram_made")
        gram_half = sem("gram_half")
        gram_scaled = sem("gram_scaled")
        gram_turned = sem("gram_turned")
        gram_added = sem("gram_added")
        half_turned = sem("half_turned")
        tail = sem("tail")
        ident_ready = sem("ident_ready")
        partners_ready = sem("partners_ready")
        member_T = sem("member_T")
        memberT_ready = sem("memberT_ready")
        mom_made = sem("mom_made")
        var_ready = sem("var_ready")
        inv_ready = sem("inv_ready")
        scale_ready = sem("scale_ready")
        shift_ready = sem("shift_ready")
        v_out = sem("v_out")
        a_head = sem("a_head")
        a_out = sem("a_out")
        stored = sem("stored")

        ident = wd[:, IDENT:IDENT + P]
        halves = [slice(h * BANK, (h + 1) * BANK) for h in range(H)]
        TH = T // H
        L = B - 1
        ACT_IMAGES = [b for b in range(B) if b % 3 == 2]
        VEC_IMAGES = [b for b in range(1, B) if b % 3 != 2]
        GROUPS = [slice(0, 1), slice(1, 3), slice(3, B)]

        def shifts_for(b):
            return next(n for n, g in enumerate(GROUPS) if b < g.stop) + 1

        def image(stack, b):
            return stack[:, bass.ds(b, 1), :].rearrange("p a n -> p (a n)")

        WHOLE = [t for t in range(T) if t not in SPLIT]

        def ahead(b, t, par):
            return (b, t, par) if t < T else (b + 1, t - T, 1 - par)

        def split_count(b, t):
            return len(SPLIT) * b + SPLIT.index(t) + 1

        def whole_count(b, t):
            return len(WHOLE) * b + WHOLE.index(t) + 1

        def run_stages(engine, stage):
            stage(0, 0, first=True, previous=False, turn=False)
            stage(1, 1, turn=False)
            with engine.Fori(0, B // 2 - 2) as i:
                stage(2 * i + 2, 0, x_count=16 * i + 32)
                stage(2 * i + 3, 1, x_count=16 * i + 32)
            stage(B - 2, 0, load_ahead=False, x_count=8 * B)
            stage(B - 1, 1, project=False)

        block = ctx.enter_context(nc.Block())

        @block.sync
        def _(sp):
            def load(b, par):
                sp.dma_start(x_all[:, b, :], x[b]).then_inc(x_in[par], 16)

            def stage(b, par, first=False, previous=True, turn=True, project=True, load_ahead=True, x_count=16):
                if project:
                    sp.wait_ge(v_proj, H * (b + 1))
                    sp.wait_ge(x_in[1 - par], x_count)
                    sp.dma_start(x_cur[:, :], x_all[:, b + 1, :]).then_inc(cur_in, 16)
                    if load_ahead:
                        load(b + 2, par)
                if previous:
                    sp.wait_ge(y_ready, H * b)
                    sp.dma_start(y_all[:, b - 1, :], y_cur[:, :]).then_inc(y_kept, 16)

            for h in range(H):
                sp.dma_start(x_all[:, 0, halves[h]], x[0][:, halves[h]]).then_inc(head_in[h], 16)
            load(1, 1)
            run_stages(sp, stage)
            sp.wait_ge(v_out, 1)
            sp.dma_start(out[0][:, halves[0]], y_all[:, 0, halves[0]]).then_inc(stored, 16)
            sp.wait_ge(a_head, 1)
            sp.dma_start(out[0][:, halves[1]], y_all[:, 0, halves[1]]).then_inc(stored, 16)
            for n, b in enumerate(VEC_IMAGES):
                sp.wait_ge(v_out, n + 2)
                sp.dma_start(out[b], y_all[:, b, :]).then_inc(stored, 16)
            sp.wait_ge(stored, 16 * (B + 1))

        @block.gpsimd
        def _(pool):
            nc.gpsimd.memset(mhalf[:, :], -0.5).then_inc(halves_set, 1)
            pool.wait_ge(halves_set, 1)

            def parts_f(b):
                for h in range(H):
                    pool.wait_ge(neg_ready, H * b + h + 1)
                    if b >= 2:
                        pool.wait_ge(scores, T * (b - 1))
                    nc.gpsimd.tensor_tensor(f_parts[b % 2][0:KP, halves[h]], fg32[0:KP, halves[h]],
                                            fg_neg[0:KP, halves[h]].bitcast(F32), ALU.add).then_inc(f_ready, 1)

            pool.wait_ge(neg_ready, H)
            pool.wait_ge(zeros_set, 4)
            nc.gpsimd.tensor_tensor(f_parts[0][0:KP, halves[1]], fg32[0:KP, halves[1]],
                                    fg_neg[0:KP, halves[1]].bitcast(F32), ALU.add).then_inc(f_ready, 1)
            for b in range(B):
                if b == 0:
                    parts_f(1)
                if b + 2 < B:
                    parts_f(b + 2)
                if b < L:
                    pool.wait_ge(sq_ready, b + 1)
                    nc.gpsimd.tensor_scalar(nsq[:, b:b + 1], stats[:, b + B:b + B + 1], NORM_FLOOR ** 2, None,
                                            ALU.max).then_inc(nsq_ready, 1)
                else:
                    pool.wait_ge(sq_ready, L + 2)
                    nc.gpsimd.tensor_scalar(nsq[:, L:B], last_sq[:, 0:1], last_sq[:, 1:2], NORM_FLOOR ** 2,
                                            ALU.add, ALU.max).then_inc(nsq_ready, 1)
                pool.wait_ge(nsq_ready, b + 1)
                nc.gpsimd.tensor_tensor(rnorm[:, b:b + 1], nsq[:, b:b + 1], mhalf[:, 0:1],
                                        ALU.pow).then_inc(rnorm_ready, 1)
            pool.wait_ge(table_in, 1)
            pool.wait_ge(var_ready, 1)
            for g in GROUPS:
                nc.gpsimd.tensor_tensor(inv[:, g], var[:, g], mhalf[:, g], ALU.pow).then_inc(inv_ready, 1)

        @block.scalar
        def _(act):
            act.dma_start(wd[:, 0:WHT], wide[:, 0:WHT]).then_inc(wfg_in, 16)
            act.dma_start(wd[:, WHT:WIDE], wide[:, WHT:WIDE]).then_inc(const_in, 16)

            act.wait_ge(halves_set, 1)
            nc.scalar.activation(inv[:, 0:1], mhalf[:, 0:1], ACT.Exp).then_inc(table_in, 1)

            def copy_fg(b, h):
                act.wait_ge(fg_proj, H * b + h + 1)
                nc.scalar.activation(fg32[:, halves[h]], w_ps[:, halves[h]], ACT.Identity,
                                     bias=wd[:, BFG:BFG + 1]).then_inc(fg_copied, 1)
                act.wait_ge(fg_copied, H * b + h + 1)
                nc.scalar.activation(fg_neg[:, halves[h]], fg32[:, halves[h]], ACT.Copy,
                                     scale=wd[:, NMASK:NMASK + 1]).then_inc(neg_ready, 1)

            def exp(b, t, par, fresh=False):
                act.wait_ge(max_ready, T * b + t + 1)
                if not fresh:
                    act.wait_ge(probs_used, T * (b - 1) + t + 1)
                nc.scalar.activation(probs[t][:, :], s_ps[t % 2][:, :], ACT.Exp, bias=nmax[:, t:t + 1],
                                     accum_out=rsum[:, t:t + 1]).then_inc(exp_done, 1)

            def high_part(b, t, par):
                act.wait_ge(exp_done, T * b + t + 1)
                nc.scalar.activation(probs_high[SPLIT.index(t)][:, :], probs[t][:, :],
                                     ACT.Copy).then_inc(high_ready, 1)

            def scale_values(b, t, par, fresh=False):
                act.wait_ge(rinv_ready, T * b + t + 1)
                if t == WHOLE[0] or fresh:
                    act.wait_ge(v_ready, H * b + 1)
                if t == next(w for w in WHOLE if w >= TH):
                    act.wait_ge(v_ready, H * b + 2)
                if not fresh:
                    act.wait_ge(probs_used, T * (b - 1) + t + 1)
                nc.scalar.activation(vnorm[t][:, :], values[par][:, t, :], ACT.Copy,
                                     scale=rinv[:, t:t + 1]).then_inc(vn_ready, 1)

            def stage(b, par, first=False, previous=True, turn=True, project=True, load_ahead=True, x_count=16):
                for t in range(T):
                    if project or t + AHEAD < T:
                        exp(*ahead(b, t + AHEAD, par), fresh=first and t + AHEAD < T)
                    if (project or t + SCALED < T) and (t + SCALED) % T in WHOLE:
                        scale_values(*ahead(b, t + SCALED, par), fresh=first and t + SCALED < T)
                    if (project or t + AHEAD < T) and (t + AHEAD) % T in SPLIT:
                        high_part(*ahead(b, t + AHEAD, par))
                    if t == 0 and previous:
                        act.wait_ge(y_ready, H * b)
                        nc.scalar.activation(squares[:, :], y_cur[:, :], ACT.Square,
                                             accum_out=stats[:, bass.ds(b - 1 + B, 1)]).then_inc(sq_ready, 1)
                    if t == 1 and project:
                        act.wait_ge(g_ready, H * (b + 1))
                        if first:
                            act.wait_ge(f_head, 1)
                        act.wait_ge(f_ready, H * b + 1)
                        copy_fg(b + 1, 0)
                    if t == 2 and project:
                        copy_fg(b + 1, 1)
                    if t == 3 and previous:
                        act.wait_ge(yT_made, b)
                        nc.scalar.activation(yT[:, :, 0:P], w_ps[:, :].rearrange("p (t c) -> p t c", c=P),
                                             ACT.Copy).then_inc(yT_high, 1)

            act.wait_ge(wfg_in, 16)
            for h in range(H):
                copy_fg(0, h)
            for t in range(AHEAD):
                exp(0, t, 0, fresh=True)
                if t > 0:
                    scale_values(0, t - 1, 0, fresh=True)
            run_stages(act, stage)

            def square(h):
                act.wait_ge(y_ready, H * L + 1 + h)
                nc.scalar.activation(squares[:, halves[h]], y_all[:, L, halves[h]], ACT.Square,
                                     accum_out=last_sq[:, h:h + 1]).then_inc(sq_ready, 1)

            square(0)
            act.wait_ge(gram_made, L)
            for h in range(H):
                act.wait_ge(yT_made, L + 1 + h)
                nc.scalar.activation(yT[:, h * TH:(h + 1) * TH, 0:P],
                                     s_ps[h][:, halves[0]].rearrange("p (t c) -> p t c", c=P),
                                     ACT.Copy).then_inc(yT_high, 1)
            square(1)
            act.wait_ge(y_kept, 16 * L)
            act.wait_ge(shift_ready, 1)
            nc.scalar.activation(y_all[:, 0, halves[1]], y_all[:, 0, halves[1]], ACT.Identity, bias=shf[:, 0:1],
                                 scale=scl[:, 0:1]).then_inc(a_head, 1)
            for n, b in enumerate(ACT_IMAGES):
                act.wait_ge(shift_ready, shifts_for(b))
                nc.scalar.activation(y_all[:, b, :], y_all[:, b, :], ACT.Identity, bias=shf[:, b:b + 1],
                                     scale=scl[:, b:b + 1]).then_inc(a_out, 1)
                act.wait_ge(a_out, n + 1)
                act.dma_start(out[b], y_all[:, b, :]).then_inc(stored, 16)

        @block.vector
        def _(dve):
            def row_max(b, t, par):
                dve.wait_ge(scores, T * b + t + 1)
                nc.vector.reduce_max(nmax[:, t:t + 1], s_ps[t % 2][:, :], AX_X, negate=True).then_inc(max_ready, 1)

            def invert_sum(b, t, par):
                dve.wait_ge(exp_done, b * T + t + 1)
                nc.vector.reciprocal(rinv[:, t:t + 1], rsum[:, t:t + 1]).then_inc(rinv_ready, 1)

            def split_parts(b, t, par):
                n = SPLIT.index(t)
                dve.wait_ge(rinv_ready, b * T + t + 1)
                nc.vector.tensor_scalar(v_high[n][:, :], values[par][:, t, :], rinv[:, t:t + 1], None,
                                        ALU.mult).then_inc(vh_ready, 1)
                dve.wait_ge(high_ready, split_count(b, t))
                nc.vector.tensor_tensor(probs_low[n][:, :], probs[t][:, :], probs_high[n][:, :].bitcast(F32),
                                        ALU.subtract).then_inc(low_ready, 1)
                dve.wait_ge(vh_ready, split_count(b, t))
                nc.vector.scalar_tensor_tensor(v_low[n][:, :], values[par][:, t, :], rinv[:, t:t + 1],
                                               v_high[n][:, :].bitcast(F32), ALU.mult,
                                               ALU.subtract).then_inc(vl_ready, 1)

            def parts(to, rows, columns, done):
                nc.vector.tensor_tensor(to[0:KP, columns], fg32[rows, columns], fg_neg[rows, columns].bitcast(F32),
                                        ALU.add).then_inc(done, 1)

            f_rows, g_rows = slice(0, KP), slice(KP, P)

            def add_value_bias(b, par, h, source):
                dve.wait_ge(v_proj, H * b + h + 1)
                bias = wd[:, BH:BH + P].rearrange("p (a c) -> p a c", a=1).to_broadcast([P, TH, P])
                nc.vector.tensor_tensor(values[par][:, h * TH:(h + 1) * TH, :],
                                        source[:, halves[h]].rearrange("p (t c) -> p t c", c=P),
                                        bias, ALU.add).then_inc(v_ready, 1)

            def residual(b, first):
                dve.wait_ge(probs_used, T * (b + 1))
                if not first:
                    dve.wait_ge(y_kept, 16 * b)
                    dve.wait_ge(sq_ready, b)
                    dve.wait_ge(yT_made, b)
                for h in range(H):
                    nc.vector.scalar_tensor_tensor(y_cur[:, halves[h]], o_ps[:, halves[h]], wd[:, GAMMA:GAMMA + 1],
                                                   image(x_all, b)[:, halves[h]], ALU.mult, ALU.add,
                                                   accum_out=sums[:, h, bass.ds(b, 1)]).then_inc(y_ready, 1)

            def low_part(tiles, source):
                nc.vector.tensor_tensor(yT[:, tiles, P:2 * P], source.rearrange("p (t c) -> p t c", c=P),
                                        yT[:, tiles, 0:P].bitcast(F32), ALU.subtract).then_inc(yT_ready, 1)

            def scale_gram(b, product):
                dve.wait_ge(gram_made, b + 1)
                dve.wait_ge(rnorm_ready, b + 1)
                nc.vector.tensor_scalar(gram_high[:, :], product[:, 0:P], rnorm[:, bass.ds(b, 1)], 0.5,
                                        ALU.mult, ALU.mult).then_inc(gram_half, 1)
                dve.wait_ge(gram_half, b + 1)
                nc.vector.scalar_tensor_tensor(gram_rows[:, :], product[:, P:2 * P], rnorm[:, bass.ds(b, 1)],
                                               gram_high[:, :], ALU.mult, ALU.add).then_inc(gram_scaled, 1)

            def add_gram(b, turned):
                dve.wait_ge(gram_turned, b + 1)
                dve.wait_ge(gram_added, b + 1)
                nc.vector.scalar_tensor_tensor(half_cos[:, :], turned, rnorm[:, bass.ds(b, 1)], half_cos[:, :],
                                               ALU.mult, ALU.add).then_inc(gram_added, 1)

            def stage(b, par, first=False, previous=True, turn=True, project=True, load_ahead=True, x_count=16):
                for t in range(T):
                    if t == 2 and turn:
                        add_gram(b - 2, w_ps[:, BANK:BANK + P])
                    if project or t + AHEAD < T:
                        row_max(*ahead(b, t + AHEAD, par))
                    if project or t + SCALED < T:
                        invert_sum(*ahead(b, t + SCALED, par))
                    if t in (4, 5) and previous:
                        h = t - 4
                        dve.wait_ge(yT_high, b)
                        low_part(slice(h * TH, (h + 1) * TH), w_ps[:, halves[h]])
                    if t == 6 and project:
                        add_value_bias(b + 1, 1 - par, 0, w_ps)
                    if t == T - 1 and project:
                        residual(b, first=first)
                    if (project or t + SCALED < T) and (t + SCALED) % T in SPLIT:
                        split_parts(*ahead(b, t + SCALED, par))
                    if t == 0 and turn:
                        scale_gram(b - 2, w_ps)
                    if t == 0 and previous:
                        add_value_bias(b, par, 1, w_ps)
                    if t in (2, 3) and project:
                        dve.wait_ge(neg_ready, H * (b + 1) + t - 1)
                        parts(g_parts[1 - par], g_rows, halves[t - 2], g_ready)

            nc.vector.memset(warm[:, :], 0.0).then_inc(warm_set, 1)
            for i in range(2):
                nc.vector.memset(f_parts[i][KP:P, :].bitcast(F32), 0.0).then_inc(zeros_set, 1)
                nc.vector.memset(g_parts[i][KP:P, :].bitcast(F32), 0.0).then_inc(zeros_set, 1)
            nc.vector.memset(half_cos[:, :], 0.0).then_inc(gram_added, 1)
            dve.wait_ge(wfg_in, 16)
            for h in range(H):
                dve.wait_ge(neg_ready, h + 1)
                parts(g_parts[0], g_rows, halves[h], g_ready)
                if h == 0:
                    parts(f_parts[0], f_rows, halves[0], f_head)
            dve.wait_ge(const_in, 16)
            for h in range(H):
                add_value_bias(0, 0, h, o_ps)
            for t in range(2):
                row_max(0, t, 0)
            invert_sum(0, 0, 0)
            row_max(0, 2, 0)
            invert_sum(0, 1, 0)
            nc.vector.tensor_copy(ident_b[:, :], ident).then_inc(ident_ready, 1)
            run_stages(dve, stage)
            for h in range(H):
                if h == 0:
                    dve.wait_ge(first_half, 1)
                else:
                    dve.wait_ge(probs_used, T * B)
                nc.vector.scalar_tensor_tensor(y_all[:, L, halves[h]], o_ps[:, halves[h]], wd[:, GAMMA:GAMMA + 1],
                                               x_all[:, L, halves[h]], ALU.mult, ALU.add,
                                               accum_out=sums[:, h, L:L + 1]).then_inc(y_ready, 1)
            scale_gram(L - 1, w_ps)
            for h in range(H):
                dve.wait_ge(yT_high, L + 1 + h)
                low_part(slice(h * TH, (h + 1) * TH), s_ps[h][:, halves[0]])
            add_gram(L - 1, w_ps[:, BANK:BANK + P])
            scale_gram(L, o_ps)
            dve.wait_ge(sq_ready, L + 2)
            nc.vector.tensor_tensor(stats[:, 2 * B - 1:2 * B], last_sq[:, 0:1], last_sq[:, 1:2],
                                    ALU.add).then_inc(sums_ready, 1)
            dve.wait_ge(y_ready, H * B)
            nc.vector.tensor_tensor(stats[:, 0:B], sums[:, 0, :], sums[:, 1, :], ALU.add).then_inc(sums_ready, 1)
            add_gram(L, o_ps[:, BANK:BANK + P])

            steps = [0]

            def step(instruction):
                steps[0] += 1
                instruction.then_inc(tail, 1)
                dve.wait_ge(tail, steps[0])

            dve.wait_ge(gram_added, B + 1)
            step(nc.vector.tensor_scalar(half_mean[:, :], half_cos[:, :], 1.0 / B, None, ALU.mult))
            dve.wait_ge(half_turned, 1)
            step(nc.vector.scalar_tensor_tensor(cos[:, :], s_ps[0][:, BANK:BANK + P], 1.0 / B, half_mean[:, :],
                                                ALU.mult, ALU.add))
            step(nc.vector.scalar_tensor_tensor(nabs[:, :], cos[:, :], -1.0, cos[:, :], ALU.mult, ALU.min))
            step(nc.vector.max(top[:, :], nabs[:, :]))
            step(nc.vector.max_index(top_at[:, :], top[:, :], nabs[:, :]))
            iota = wd[:, IOTA:IOTA + P].rearrange("p (a c) -> p a c", a=1).to_broadcast([P, PARTNERS, P])
            at = top_at[:, 1:PARTNERS + 1].rearrange("p (k a) -> p k a", a=1).to_broadcast([P, PARTNERS, P])
            nc.vector.tensor_tensor(partner[:, :, :], iota, at, ALU.is_equal).then_inc(partners_ready, 1)
            dve.wait_ge(sums_ready, 2)
            nc.vector.tensor_scalar(shares[:, :], stats[:, :], 1.0 / ((PARTNERS + 1) * N), None,
                                    ALU.mult).then_inc(sums_ready, 1)
            dve.wait_ge(member_T, 1)
            nc.vector.tensor_copy(memberT[:, :], w_ps[:, 0:P]).then_inc(memberT_ready, 1)
            dve.wait_ge(mom_made, 1)
            step(nc.vector.tensor_copy(mean[:, :], o_ps[:, 0:B]))
            step(nc.vector.tensor_tensor(msq[:, :], mean[:, :], mean[:, :], ALU.mult))
            nc.vector.scalar_tensor_tensor(var[:, :], o_ps[:, B:2 * B], GN_EPS, msq[:, :], ALU.add,
                                           ALU.subtract).then_inc(var_ready, 1)
            step(nc.vector.tensor_scalar(msc[:, :], mean[:, :], wd[:, GNG:GNG + 1], -1.0, ALU.mult, ALU.mult))
            dve.wait_ge(y_kept, 16 * L)
            for n, g in enumerate(GROUPS):
                dve.wait_ge(inv_ready, n + 1)
                nc.vector.tensor_scalar(scl[:, g], inv[:, g], wd[:, GNG:GNG + 1], None,
                                        ALU.mult).then_inc(scale_ready, 1)
                if n == 0:
                    nc.vector.tensor_scalar(shf[:, g], msc[:, g], inv[:, g], wd[:, GNB:GNB + 1], ALU.mult,
                                            ALU.add).then_inc(shift_ready, 1)
                else:
                    step(nc.vector.tensor_tensor(minv[:, g], inv[:, g], msc[:, g], ALU.mult))
                    nc.vector.tensor_scalar(shf[:, g], minv[:, g], wd[:, GNB:GNB + 1], None,
                                            ALU.add).then_inc(shift_ready, 1)
                dve.wait_ge(scale_ready, n + 1)
                dve.wait_ge(shift_ready, n + 1)
                if n == 0:
                    nc.vector.tensor_scalar(y_all[:, 0, halves[0]], y_all[:, 0, halves[0]], scl[:, 0:1], shf[:, 0:1],
                                            ALU.mult, ALU.add).then_inc(v_out, 1)
                for b in VEC_IMAGES:
                    if shifts_for(b) == n + 1:
                        nc.vector.tensor_scalar(y_all[:, b, :], y_all[:, b, :], scl[:, b:b + 1], shf[:, b:b + 1],
                                                ALU.mult, ALU.add).then_inc(v_out, 1)

        @block.tensor
        def _(pe):
            def keep_warm(to):
                for _ in range(WARM_UPS):
                    nc.tensor.matmul(to[:, halves[0]], warm[:, 0:P], warm[:, :], start=True, stop=True)

            def project_fg(b, h):
                return nc.tensor.matmul(w_ps[:, halves[h]], wd[:, WFG:WFG + P], image(x_all, b)[:, halves[h]],
                                        start=True, stop=True)

            def project_values(source, to, h):
                for t in range(h * TH, (h + 1) * TH):
                    last = nc.tensor.matmul(to[:, t * P:(t + 1) * P], source[:, t * P:(t + 1) * P],
                                            wd[:, WHT:WHT + P], start=True, stop=True)
                last.then_inc(v_proj, 1)

            def score(t, par):
                for h in halves:
                    last = nc.tensor.matmul(s_ps[t % 2][:, h], f_parts[par][:, t * P:(t + 1) * P],
                                            g_parts[par][:, h], start=True, stop=True)
                last.then_inc(scores, 1)

            def attend(b, t, after=None, halves_apart=False):
                if t in SPLIT:
                    pe.wait_ge(vl_ready, split_count(b, t))
                else:
                    pe.wait_ge(vn_ready, whole_count(b, t))
                for h in range(H):
                    if after is not None:
                        pe.wait_ge(y_ready, H * (after - 1) + h + 1)
                    if t in SPLIT:
                        n = SPLIT.index(t)
                        products = [(v_high[n], probs_high[n]), (v_low[n], probs_high[n]), (v_high[n], probs_low[n])]
                    else:
                        products = [(vnorm[t], probs[t])]
                    for n, (weights, rows) in enumerate(products):
                        last = nc.tensor.matmul(o_ps[:, halves[h]], weights[:, :], rows[:, halves[h]],
                                                start=(t == 0 and n == 0),
                                                stop=(t == T - 1 and n == len(products) - 1))
                    if h == 0 and halves_apart:
                        last.then_inc(first_half, 1)
                last.then_inc(probs_used, 1)

            def transposes(source, to, tiles, first=0):
                for t in tiles:
                    last = nc.tensor.transpose(to[:, (t - first) * P:(t - first + 1) * P],
                                               source[:, t * P:(t + 1) * P], ident)
                return last

            def gram(to, tiles):
                for t in tiles:
                    last = nc.tensor.matmul(to[:, 0:2 * P], yT[:, t, 0:P], yT[:, t, :], start=(t == 0),
                                            stop=(t == T - 1))
                return last

            def turn_gram(b, to):
                pe.wait_ge(gram_scaled, b + 1)
                nc.tensor.transpose(to, gram_rows[:, :], ident).then_inc(gram_turned, 1)

            def stage(b, par, first=False, previous=True, turn=True, project=True, load_ahead=True, x_count=16):
                for t in range(T):
                    if project or t + AHEAD < T:
                        pe.wait_ge(exp_done, T * b + t + AHEAD - 1)
                        if t + AHEAD == T:
                            pe.wait_ge(g_ready, H * (b + 2))
                            pe.wait_ge(f_ready, H * b + 2)
                        if t + AHEAD == TH:
                            pe.wait_ge(f_ready, H * b + 1)
                        _, tile, its_par = ahead(b, t + AHEAD, par)
                        score(tile, its_par)
                    if t == 4 and previous:
                        if project:
                            pe.wait_ge(fg_copied, H * (b + 2))
                        transposes(y_cur, w_ps, range(TH, T)).then_inc(yT_made, 1)
                    if first and t == 0:
                        pe.wait_ge(v_ready, H)
                    attend(b, t, b if t == 0 and previous else None,
                           halves_apart=not project and t == T - 1)
                    if t == 1 and project and not first:
                        if turn:
                            pe.wait_ge(gram_scaled, b - 1)
                        pe.wait_ge(x_in[1 - par], x_count)
                        project_fg(b + 1, 0).then_inc(fg_proj, 1)
                    if t == 1 and previous:
                        pe.wait_ge(v_ready, H * (b + 1))
                    if t == 1 and turn:
                        turn_gram(b - 2, w_ps[:, BANK:BANK + P])
                    if t == 2 and project and not first:
                        if turn:
                            pe.wait_ge(gram_added, b)
                        project_fg(b + 1, 1).then_inc(fg_proj, 1)
                    if t == 3 and previous:
                        if project:
                            pe.wait_ge(fg_copied, H * (b + 1) + 1)
                        else:
                            pe.wait_ge(gram_added, b)
                        transposes(y_cur, w_ps, range(TH))
                    if t in (5, 6) and project:
                        pe.wait_ge(cur_in, 16 * (b + 1))
                        if previous:
                            pe.wait_ge(yT_ready, H * (b - 1) + t - 4)
                        else:
                            pe.wait_ge(fg_copied, 2 * H)
                        project_values(x_cur, w_ps, t - 5)
                if previous:
                    if project:
                        pe.wait_ge(v_ready, H * (b + 1) + 1)
                    pe.wait_ge(yT_ready, H * b)
                    gram(w_ps, range(T)).then_inc(gram_made, 1)

            pe.wait_ge(warm_set, 1)
            keep_warm(o_ps)
            pe.wait_ge(wfg_in, 16)
            for h in range(H):
                pe.wait_ge(head_in[h], 16)
                project_fg(0, h).then_inc(fg_proj, 1)
            pe.wait_ge(const_in, 16)
            for h in range(H):
                project_values(x_all[:, 0, :], o_ps, h)
            pe.wait_ge(zeros_set, 4)
            pe.wait_ge(g_ready, H)
            pe.wait_ge(f_head, 1)
            score(0, 0)
            score(1, 0)
            pe.wait_ge(x_in[1], 16)
            pe.wait_ge(fg_copied, H)
            for h in range(H):
                project_fg(1, h).then_inc(fg_proj, 1)
            pe.wait_ge(exp_done, 1)
            score(2, 0)
            run_stages(pe, stage)
            for h in range(H):
                pe.wait_ge(y_ready, H * L + 1 + h)
                transposes(y_all[:, L, :], s_ps[h], range(h * TH, (h + 1) * TH), first=h * TH).then_inc(yT_made, 1)
            turn_gram(L - 1, w_ps[:, BANK:BANK + P])
            for h in range(H):
                pe.wait_ge(yT_ready, H * L + 1 + h)
                last = gram(o_ps, range(h * TH, (h + 1) * TH))
            last.then_inc(gram_made, 1)
            turn_gram(L, o_ps[:, BANK:BANK + P])
            pe.wait_ge(gram_added, B + 1)
            nc.tensor.transpose(s_ps[0][:, BANK:BANK + P], half_cos[:, :], ident).then_inc(half_turned, 1)
            pe.wait_ge(ident_ready, 1)
            nc.tensor.matmul(w_ps[:, 0:P], ident_b[:, :], ident_b[:, :], start=True, stop=False)
            pe.wait_ge(partners_ready, 1)
            for k in range(PARTNERS):
                last = nc.tensor.matmul(w_ps[:, 0:P], partner[:, k, :], ident_b[:, :], start=False,
                                        stop=(k == PARTNERS - 1))
            last.then_inc(member_T, 1)
            pe.wait_ge(memberT_ready, 1)
            pe.wait_ge(sums_ready, 3)
            nc.tensor.matmul(o_ps[:, 0:2 * B], memberT[:, :], shares[:, :], start=True, stop=True).then_inc(mom_made, 1)


def kernel(x, L0_conv_Wf, L0_conv_bf, L0_conv_Wg, L0_conv_bg, L0_conv_Wh, L0_conv_bh, L0_conv_gamma,
           L1_conv_gamma, L1_conv_beta):
    import concourse.bacc as bacc
    from concourse.bass_utils import run_bass_kernel_spmd

    f32 = np.float32
    a = {k: np.asarray(v) for k, v in locals().items() if k.startswith(("x", "L"))}
    B, C, Hh, Ww = a["x"].shape
    CB = a["L0_conv_Wf"].shape[0]
    wide = np.zeros((P, WIDE), f32)
    wide[:, WFG:WFG + P] = np.concatenate([a["L0_conv_Wf"].T] * 4 + [a["L0_conv_Wg"].T] * 4, axis=1)
    wide[:, WHT:WHT + P] = a["L0_conv_Wh"].T
    wide[:, BH:BH + P] = a["L0_conv_bh"][None, :]
    wide[:, IDENT:IDENT + P] = np.eye(P, dtype=f32)
    wide[:, IOTA:IOTA + P] = np.arange(P, dtype=f32)[None, :]
    wide[:, BFG] = np.concatenate([a["L0_conv_bf"]] * 4 + [a["L0_conv_bg"]] * 4)
    low = np.repeat(np.array([0, 1, 0, 1, 0, 0, 1, 1], f32), CB)
    wide[:, NMASK] = np.where(low > 0, f32(-1), f32(0))
    wide[:, GAMMA] = a["L0_conv_gamma"][0]
    wide[:, GNG] = a["L1_conv_gamma"]
    wide[:, GNB] = a["L1_conv_beta"]
    arrays = {"x_dram": np.ascontiguousarray(a["x"].reshape(B, C, Hh * Ww)), "wide_dram": wide}

    nc = bacc.Bacc("TRN2", target_bir_lowering=False, num_devices=1)
    args = [nc.dram_tensor(k, v.shape, F32, kind="ExternalInput").ap() for k, v in arrays.items()]
    args.append(nc.dram_tensor("out_dram", (B, C, Hh * Ww), F32, kind="ExternalOutput").ap())
    build(nc, *args)
    r = run_bass_kernel_spmd(nc, [arrays], core_ids=[0])
    return r.results[0]["out_dram"].reshape(B, C, Hh, Ww)
```
